# Optimizing a Trainium2 kernel written in Bass

```python
import numpy as np
import jax
import jax.numpy as jnp

def _softmax(x, axis=-1):
    return jax.nn.softmax(x, axis=axis)

def _gelu(x):
    return jax.nn.gelu(x, approximate=True)

def _silu(x):
    return jax.nn.silu(x)

def _sigmoid(x):
    return jax.nn.sigmoid(x)

def _layernorm(x, axis=-1, eps=1e-05):
    m = jnp.mean(x, axis=axis, keepdims=True)
    v = jnp.var(x, axis=axis, keepdims=True)
    return (x - m) / jnp.sqrt(v + eps)

def _scatter_add(tgt, idx, src, axis=0):
    return tgt.at[idx].add(src)

def _segment_sum(src, seg, n):
    return jax.ops.segment_sum(src, seg, n)
kernel_name = 'mk_cond_resid_d2_seqx_r4_52c477'

def setup_inputs(seed: int=0):
    np.random.seed(seed)
    _w = jnp.asarray

    def _rec_inputs():
        import jax
        import jax.numpy as jnp
        _rk = jax.random.key(seed)
        x = -0.000125 + 0.9999 * jax.random.normal(jax.random.fold_in(_rk, 1), (8, 256, 1024), jnp.float32)
        _lenS = 256 - jax.random.randint(jax.random.fold_in(_rk, 7), (8,), 0, max(1, 256 // 4) + 1, jnp.int32)
        _lenS2 = 256 - jax.random.randint(jax.random.fold_in(_rk, 8), (8,), 0, max(1, 256 // 4) + 1, jnp.int32)
        itok_B_0_7 = jax.random.randint(jax.random.fold_in(_rk, 11), (8,), 0, 8, jnp.int32)
        itok_B_0_15 = jax.random.randint(jax.random.fold_in(_rk, 12), (8,), 0, 16, jnp.int32)
        return (x, itok_B_0_7, itok_B_0_15)
    x, itok_B_0_7, itok_B_0_15 = _rec_inputs()

    def _L0_cond_setup():
        import jax, jax.numpy as jnp
        import numpy as np
        TOP_K = 2
        LANG_BIAS = 5.0
        SCALING = 32.0 / 16.0
        LANGUAGE_PAD_ID = -1
        key = jax.random.key(seed)
        ks = jax.random.split(key, 6)
        B, T, D, O, E, R = (4, 512, 1024, 1024, 8, 16)
        x = jax.random.normal(ks[0], (B, T, D), dtype=jnp.float32)
        language_ids = jax.random.randint(ks[1], (B,), 0, E).astype(jnp.int64)
        W = jax.random.normal(ks[2], (O, D), dtype=jnp.float32) * (1.0 / np.sqrt(D))
        Wr = jax.random.normal(ks[3], (E, D), dtype=jnp.float32) * (1.0 / np.sqrt(D))
        A = jax.random.normal(ks[4], (E, R, D), dtype=jnp.float32) * (1.0 / np.sqrt(D))
        Bm = jax.random.normal(ks[5], (O, R), dtype=jnp.float32) * 0.0
        Bm = jnp.broadcast_to(Bm, (E, O, R)) + jax.random.normal(ks[5], (E, O, R), dtype=jnp.float32) * 0.02
        return {'x': x, 'language_ids': language_ids, 'W': W, 'Wr': Wr, 'A': A, 'B': Bm}
    _L0_cond_all = _L0_cond_setup()
    _L0_cond_in = {k: v for k, v in _L0_cond_all.items() if k in ('W', 'Wr', 'A', 'B')}
    del _L0_cond_all

    def _L1_cond_setup():
        import jax, jax.numpy as jnp
        import numpy as np
        MAX_LORAS = 16
        IN, OUT = (1024, 1024)
        B, S = (8, 512)
        key = jax.random.key(seed)
        k1, k2, k3 = jax.random.split(key, 3)
        x = jax.random.normal(k1, (B, S, IN), dtype=jnp.float32)
        adapter_ids = jax.random.randint(k2, (B,), 0, MAX_LORAS)
        weight = jax.random.normal(k3, (MAX_LORAS, OUT, IN), dtype=jnp.float32) * 0.02
        return {'x': x, 'adapter_ids': adapter_ids, 'weight': weight}
    _L1_cond_all = _L1_cond_setup()
    _L1_cond_in = {k: v for k, v in _L1_cond_all.items() if k in ('weight',)}
    del _L1_cond_all
    return {'x': x, 'itok_B_0_7': itok_B_0_7, 'itok_B_0_15': itok_B_0_15, 'L0_cond_W': _L0_cond_in['W'], 'L0_cond_Wr': _L0_cond_in['Wr'], 'L0_cond_A': _L0_cond_in['A'], 'L0_cond_B': _L0_cond_in['B'], 'L1_cond_weight': _L1_cond_in['weight']}

def reference(x, itok_B_0_7, itok_B_0_15, L0_cond_W, L0_cond_Wr, L0_cond_A, L0_cond_B, L1_cond_weight):
    import jax
    import jax.numpy as jnp

    def _L0_cond_ref(x, language_ids, W, Wr, A, B):
        import jax, jax.numpy as jnp
        import numpy as np
        TOP_K = 2
        LANG_BIAS = 5.0
        SCALING = 32.0 / 16.0
        LANGUAGE_PAD_ID = -1
        base = jnp.einsum('btd,od->bto', x, W)
        E = Wr.shape[0]
        logits = jnp.einsum('btd,ed->bte', x.astype(jnp.float32), Wr.astype(jnp.float32))
        expert_targets = language_ids
        valid = expert_targets >= 0
        tgt = jnp.where(valid, expert_targets, 0)
        bias = jax.nn.one_hot(tgt, E, dtype=logits.dtype) * LANG_BIAS
        bias = jnp.where(valid[:, None], bias, 0.0)
        logits = logits + bias[:, None, :]
        topw, topi = jax.lax.top_k(logits, TOP_K)
        weights = jax.nn.softmax(topw, axis=-1)
        gates = jnp.sum(jax.nn.one_hot(topi, E, dtype=weights.dtype) * weights[..., None], axis=-2)
        gates = gates.astype(x.dtype)
        h = jnp.einsum('btd,erd->bter', x, A)
        lora_out = jnp.einsum('bter,bte,eor->bto', h, gates, B)
        return base + SCALING * lora_out

    def _L1_cond_ref(x, adapter_ids, weight):
        import jax, jax.numpy as jnp
        import numpy as np
        MAX_LORAS = 16
        IN, OUT = (1024, 1024)
        B, S = (8, 512)
        w = weight[adapter_ids]
        return jnp.einsum('bsi,boi->bso', x, w)
    x = x + _L0_cond_ref(x, itok_B_0_7, L0_cond_W, L0_cond_Wr, L0_cond_A, L0_cond_B)
    x = x + _L1_cond_ref(x, itok_B_0_15, L1_cond_weight)
    return x

_drawn_inputs = setup_inputs


def setup_inputs(seed=0):
    import zlib

    import numpy as np

    out = dict(_drawn_inputs(seed))
    spreads = {}
    factors = {'L0_cond_Wr': 4.977}
    for name, (base, spread) in spreads.items():
        noise = np.random.default_rng([zlib.crc32(name.encode()), seed]).standard_normal(out[name].shape)
        drawn = base * np.exp(spread * noise) if base else spread * noise
        out[name] = jnp.asarray(drawn.astype(out[name].dtype))
    for name, factor in factors.items():
        out[name] = (out[name] * factor).astype(out[name].dtype)
    return out
```

```python
import concourse.bass as bass
from concourse import mybir
from contextlib import ExitStack


def cond_resid_kernel(nc, x, lang_ids, adapter_ids, w0, wr, a, b, w1, out):
    F32 = mybir.dt.float32
    F32R = mybir.dt.float32r
    I32 = mybir.dt.int32
    U32 = mybir.dt.uint32
    ALU = mybir.AluOpType
    ACT = mybir.ActivationFunctionType

    NB, T, D = x.shape
    E, R, _ = a.shape
    NA = w1.shape[0]
    P = 128
    Q = 4
    S = P // Q
    DQ = D // Q
    M = D // P
    CH = 512
    NCH = NB * T // CH
    BPC = CH // T
    XT = CH // P
    TT = T // P
    HALF = 512
    KH = HALF // P
    NH = BPC * M // KH
    ER = E * R
    FC = ER + E
    LANG_BIAS = 5.0
    SCALING = 2.0

    WPC = M + BPC * M
    GROUPS = 3
    RING = GROUPS * KH
    RAW = 4
    BANKS = 4
    OUTS = 4
    L1_OUTS = NH * TT
    assert WPC % RING == 0 and ER == P and M % BANKS == 0 and L1_OUTS % OUTS == 0

    AHEAD = 7
    FIRST = [("x", 0), ("a", 0), ("x", 1), ("x", 2), ("x", 3)] + [("w", n) for n in range(AHEAD)]
    DURING_GATES = [("w", n) for n in range(AHEAD + 1, AHEAD + 4)]
    AFTER_L0 = [[], [("w", 11), ("w", 12)], [("w", 13), ("w", 14)], [("w", 15)], [("w", 16)], [("w", 17)],
                [("w", 18)], []]

    def after_l1(j, last):
        if last:
            return [[("w", 19)], [("w", 20), ("w", 21), ("w", 22)], [("w", 23)], []][j]
        return [[("w", 19), ("x", 0), ("x", 1), ("x", 2)], [("x", 3), ("w", 20), ("w", 21), ("w", 22)],
                [("w", 23), ("w", 24), ("w", 25), ("w", 26)], [("w", 27), ("w", 28), ("w", 29), ("w", 30)]][j]

    def body_order(last):
        return ([("w", AHEAD)] + DURING_GATES + [t for l in AFTER_L0 for t in l] +
                [t for j in range(NH) for t in after_l1(j, last)])

    N_FIRST = len(FIRST)
    N_BODY = len(body_order(False))
    assert N_FIRST % RAW == 0 and N_BODY % RAW == 0 and N_BODY == WPC + XT
    POS = {False: {t: i for i, t in enumerate(body_order(False))},
           True: {t: i for i, t in enumerate(body_order(True))}}
    FIRST_POS = {t: i for i, t in enumerate(FIRST)}

    x_rows = x.rearrange("n t d -> (n t) d")
    out_rows = out.rearrange("n t d -> (n t) d")
    a_rows = a.rearrange("e r d -> (e r) d")
    w1_rows = w1.rearrange("n o i -> (n o) i")
    b_view = b.rearrange("e (p o) r -> p e (o r)", p=P)

    ctx = ExitStack()
    with ctx:
        def sb(name, shape, dt=F32):
            return ctx.enter_context(nc.sbuf_tensor(name, shape, dt))

        def pb(name, shape):
            return ctx.enter_context(nc.psum_tensor(name, shape, F32))

        def sem(name):
            return ctx.enter_context(nc.semaphore(name))

        xT_hi, xT_lo = sb("xT_hi", [P, M, CH], F32R), sb("xT_lo", [P, M, CH], F32R)
        x1T_hi, x1T_lo = sb("x1T_hi", [P, M, CH], F32R), sb("x1T_lo", [P, M, CH], F32R)
        w_hi, w_lo = sb("w_hi", [P, GROUPS, M, HALF], F32R), sb("w_lo", [P, GROUPS, M, HALF], F32R)
        fac_hi, fac_lo = sb("fac_hi", [P, M, FC], F32R), sb("fac_lo", [P, M, FC], F32R)
        bT_hi, bT_lo = sb("bT_hi", [ER, D], F32R), sb("bT_lo", [ER, D], F32R)
        gT_hi, gT_lo = sb("gT_hi", [ER, CH], F32R), sb("gT_lo", [ER, CH], F32R)
        raw = sb("raw", [P, RAW, D])
        turned = sb("turned", [P, 2, M, P])
        out_stage = sb("out_stage", [P, OUTS, HALF])
        b_raw = out_stage[:, 0:2, :].rearrange("p s (e f) -> p (s e) f", f=M * R)
        b_sorted = out_stage[:, 2:4, :].rearrange("p s (o f) -> p (s o) f", f=ER)
        wr_turned = sb("wr_turned", [P, M, S])
        ident = sb("ident", [P, P])
        iota_i = sb("iota_i", [P, E], I32)
        iota_f = sb("iota_f", [P, E])
        lang_i = sb("lang_i", [P, NB], I32)
        lang_f = sb("lang_f", [P, NB])
        bias = sb("bias", [P, NB, E])
        adapters = sb("adapters", [1, NB], I32)
        logits = sb("logits", [P, XT, E])
        top = sb("top", [P, XT, 8])
        top_i = sb("top_i", [P, XT, 8], U32)
        pick = sb("pick", [P, XT, 2])
        largest = sb("largest", [P, XT])
        drop = sb("drop", [P, XT])
        second = sb("second", [P, XT])
        total = sb("total", [P, XT])
        share = sb("share", [P, XT])
        gate1 = sb("gate1", [P, XT])
        gate2 = sb("gate2", [P, XT])
        hot1 = sb("hot1", [P, XT, E])
        hot2 = sb("hot2", [P, XT, E])
        gates = sb("gates", [P, XT, E])
        gated = sb("gated", [P, XT, ER])
        wr_raw = gated[:, 0:2, :].rearrange("p j f -> p (j f)")

        h_ps = pb("h_ps", [P, XT, 256])
        gT_ps = pb("gT_ps", [ER, CH])
        out_ps = pb("out_ps", [P, BANKS, HALF])
        bT_ps = out_ps[:, BANKS - 2:BANKS, :].rearrange("p k f -> p (k f)")

        raw_loaded = [sem(f"raw_loaded{s}") for s in range(RAW)]
        small_loaded = sem("small_loaded")
        b_loaded = sem("b_loaded")
        b_sorted_done = sem("b_sorted_done")
        adapters_loaded = sem("adapters_loaded")
        wr_zeroed = sem("wr_zeroed")
        consts = sem("consts")
        ones_added = sem("ones_added")
        transposed = sem("transposed")
        wr_transposed = sem("wr_transposed")
        hi_done = sem("hi_done")
        x_done = sem("x_done")
        w_done = sem("w_done")
        fac_hi_done = sem("fac_hi_done")
        fac_done = sem("fac_done")
        bT_turned = sem("bT_turned")
        bT_hi_done = sem("bT_hi_done")
        bT_done = sem("bT_done")
        w0_used = sem("w0_used")
        h_ready = sem("h_ready")
        gate_steps = sem("gate_steps")
        drop_ready = sem("drop_ready")
        second_ready = sem("second_ready")
        gated_ready = sem("gated_ready")
        gT_turned = sem("gT_turned")
        gT_hi_done = sem("gT_hi_done")
        gT_done = sem("gT_done")
        l0_ready = sem("l0_ready")
        x1_hi_done = sem("x1_hi_done")
        x1_done = sem("x1_done")
        l1_ready = sem("l1_ready")
        l1_copied = sem("l1_copied")
        stored = [sem(f"stored{s}") for s in range(OUTS)]
        setup = sem("setup")

        GATE_STEPS = 9

        def place(item, ch, last):
            return FIRST_POS[item] if ch is None else ch * N_BODY + (N_FIRST + POS[last][item])

        def slot(item, ch, last, n):
            return (FIRST_POS[item] if ch is None else POS[last][item]) % n

        def fills(item, ch, last):
            if ch is None:
                return FIRST_POS[item] // RAW + 1
            return ch * (N_BODY // RAW) + (N_FIRST // RAW + POS[last][item] // RAW + 1)

        def base(ch):
            return 0 if ch is None else ch

        def ring(t, n):
            s = n % RING
            return t[:, s // KH, :, (s % KH) * P:(s % KH + 1) * P]

        def dest(hi, item):
            kind, n = item
            if kind == "x":
                return (xT_hi if hi else xT_lo)[:, :, n * P:(n + 1) * P]
            if kind == "a":
                return (fac_hi if hi else fac_lo)[:, :, 0:ER]
            return ring(w_hi if hi else w_lo, n)

        def bT_slices(q):
            src = bT_ps.rearrange("p (o q m s) -> p q m s o", o=M, q=Q, m=M)[:, q]
            return src, lambda t: t[:].rearrange("p (m q s o) -> p q m s o", m=M, q=Q, o=M)[:, q]

        block = ctx.enter_context(nc.Block())

        @block.sync
        def _(sp):
            def rows(item, ch, ids):
                kind, n = item
                if kind == "a":
                    return a_rows[:, :].rearrange("(q s) d -> s q d", s=S)
                if kind == "x":
                    t0 = n * P if ch is None else ch * CH + (CH + n * P)
                    return x_rows[bass.ds(t0, P), :].rearrange("(q s) d -> s q d", s=S)
                if n < M or n >= WPC:
                    return w0.rearrange("(q m s) d -> m s q d", m=M, s=S)[n % WPC]
                row, m = (n - M) // M, (n - M) % M
                return w1_rows[bass.ds(ids[row] * D, D), :].rearrange("(q m s) d -> m s q d", m=M, s=S)[m]

            def load(item, ch, last, ids=None):
                s = slot(item, ch, last, RAW)
                n = place(item, ch, last)
                if ch is not None or n >= RAW:
                    sp.wait_ge(transposed, n - (RAW - 1))
                src = rows(item, ch, ids)
                for c in range(Q):
                    sp.dma_start(raw[c * S:(c + 1) * S, s, :].rearrange("p (q j) -> p q j", q=Q),
                                 src[:, :, c * DQ:(c + 1) * DQ]).then_inc(raw_loaded[s], 16)

            for item in FIRST:
                load(item, None, False)
            sp.wait_ge(adapters_loaded, 16)

            def body(ch, last):
                ids = [sp.value_load(adapters[0:1, bass.ds(ch * BPC + r, 1)], min_val=0, max_val=NA - 1)
                       for r in range(BPC)]
                for item in body_order(last):
                    load(item, ch, last, ids)

            with sp.Fori(0, NCH - 1) as ch:
                body(ch, False)
            body(NCH - 1, True)

        @block.gpsimd
        def _(pool):
            nc.gpsimd.memset(wr_raw, 0.0).then_inc(wr_zeroed, 1)
            nc.gpsimd.memset(ident[:], 0.0).then_inc(consts, 1)
            nc.gpsimd.iota(iota_i[:], [[1, E]], base=0, channel_multiplier=0).then_inc(consts, 1)
            pool.wait_ge(consts, 1)
            nc.gpsimd.affine_select(out=ident[:], in_=ident[:], compare_op=ALU.not_equal, fill=1.0, base=0,
                                    pattern=[[-1, P]], channel_multiplier=1).then_inc(consts, 1)
            pool.wait_ge(consts, 3)

            pool.wait_ge(b_loaded, 16)
            nc.gpsimd.tensor_copy(b_sorted.rearrange("p o (e r) -> p e o r", e=E),
                                  b_raw.rearrange("p e (o r) -> p e o r", r=R)).then_inc(b_sorted_done, 1)

            def add_ones(item, ch, last):
                kind, n = item
                if kind != "w":
                    return
                m = n % WPC % M
                s = slot(item, ch, last, RAW)
                spot = raw[:, s, :].rearrange("p (q j) -> p q j", q=Q)[:, :, m * S:(m + 1) * S]
                pool.wait_ge(raw_loaded[s], fills(item, ch, last) * (Q * 16))
                nc.gpsimd.tensor_tensor(spot, spot, ident[:].rearrange("p (q j) -> p q j", q=Q), ALU.add)\
                    .then_inc(ones_added, 1)

            for item in FIRST:
                add_ones(item, None, False)

            def body(ch, last):
                for item in body_order(last):
                    add_ones(item, ch, last)

            with pool.Fori(0, NCH - 1) as ch:
                body(ch, False)
            body(NCH - 1, True)

        @block.vector
        def _(dve):
            def two_before(item, ch, last):
                order, at = (FIRST, FIRST_POS[item]) if ch is None else (body_order(last), POS[last][item])
                return order[at - 2] if at >= 2 else None if ch is None else ("w", AHEAD - 2 + at)

            def made(item, ch):
                if item is None:
                    return
                kind, n = item
                if kind == "w":
                    dve.wait_ge(w_done, base(ch) * WPC + (n + 1))
                elif kind == "x":
                    dve.wait_ge(x_done, n + 1 if ch is None else ch * XT + (XT + n + 1))
                else:
                    dve.wait_ge(fac_done, 1)

            def turn(item, ch, last):
                kind, n = item
                s = slot(item, ch, last, RAW)
                if kind == "w":
                    dve.wait_ge(ones_added, base(ch) * WPC + (n + 1))
                else:
                    dve.wait_ge(raw_loaded[s], fills(item, ch, last) * (Q * 16))
                made(two_before(item, ch, last), ch)
                nc.vector.transpose(turned[:, slot(item, ch, last, 2)].rearrange("p m (q s) -> p q m s", q=Q),
                                    raw[:, s, :].rearrange("p (q m j) -> p q m j", q=Q, m=M))\
                    .then_inc(transposed, 1)

            def low(item, ch, last):
                kind, n = item
                dve.wait_ge(hi_done, place(item, ch, last) + 1)
                nc.vector.tensor_tensor(dest(False, item), turned[:, slot(item, ch, last, 2)],
                                        dest(True, item).bitcast(F32), ALU.subtract)\
                    .then_inc({"x": x_done, "w": w_done, "a": fac_done}[kind], 1)

            def make(items, ch, last):
                for before, item in zip([None] + items, items + [None]):
                    if item:
                        turn(item, ch, last)
                    if before:
                        low(before, ch, last)

            make(FIRST[0:2], None, False)
            dve.wait_ge(small_loaded, (Q + 1) * 16)
            nc.vector.transpose(wr_turned[:], wr_raw.rearrange("p (m j) -> p m j", m=M)).then_inc(wr_transposed, 1)
            dve.wait_ge(fac_hi_done, 1)
            nc.vector.tensor_tensor(fac_lo[:, :, ER:FC], wr_turned[:, :, 0:E], fac_hi[:, :, ER:FC].bitcast(F32),
                                    ALU.subtract).then_inc(fac_done, 1)
            make(FIRST[2:6], None, False)
            dve.wait_ge(consts, 3)
            nc.vector.tensor_copy(iota_f[:], iota_i[:]).then_inc(setup, 1)
            nc.vector.tensor_copy(lang_f[:], lang_i[:]).then_inc(setup, 1)
            dve.wait_ge(setup, 2)
            nc.vector.tensor_tensor(bias[:], iota_f[:].unsqueeze(1).to_broadcast([P, NB, E]),
                                    lang_f[:].unsqueeze(2).to_broadcast([P, NB, E]), ALU.is_equal).then_inc(setup, 1)
            dve.wait_ge(setup, 3)
            nc.vector.tensor_scalar(bias[:], bias[:], LANG_BIAS, None, ALU.mult).then_inc(setup, 1)
            dve.wait_ge(setup, 4)
            dve.wait_ge(bT_hi_done, Q)
            for q in range(Q):
                src, dst = bT_slices(q)
                nc.vector.tensor_tensor(dst(bT_lo), src, dst(bT_hi).bitcast(F32), ALU.subtract).then_inc(bT_done, 1)
            make(FIRST[6:], None, False)

            def make_gates(ch):
                at = lambda k: ch * GATE_STEPS + k
                dve.wait_ge(h_ready, ch + 1)
                nc.vector.tensor_tensor(
                    logits[:].rearrange("p (r t) e -> p r t e", r=BPC),
                    h_ps[:, :, ER:FC].rearrange("p (r t) e -> p r t e", r=BPC),
                    bias[:, bass.ds(ch * BPC, BPC), :].unsqueeze(2).to_broadcast([P, BPC, TT, E]),
                    ALU.add).then_inc(gate_steps, 1)
                dve.wait_ge(gate_steps, at(1))
                nc.vector.tensor_reduce(largest[:], logits[:], mybir.AxisListType.X, ALU.max)
                for j in range(XT):
                    last_max = nc.vector.max(top[:, j, :], logits[:, j, :])
                last_max.then_inc(gate_steps, 1)
                dve.wait_ge(gate_steps, at(2))
                nc.vector.tensor_tensor(drop[:], top[:, :, 1], largest[:], ALU.subtract).then_inc(drop_ready, 1)
                for j in range(XT):
                    last_index = nc.vector.max_index(top_i[:, j, :], top[:, j, :], logits[:, j, :])
                last_index.then_inc(gate_steps, 1)
                dve.wait_ge(gate_steps, at(3))
                nc.vector.tensor_copy(pick[:], top_i[:, :, 0:2]).then_inc(gate_steps, 1)
                dve.wait_ge(second_ready, ch + 1)
                nc.vector.tensor_scalar(total[:], second[:], 1.0, None, ALU.add).then_inc(gate_steps, 1)
                dve.wait_ge(gate_steps, at(5))
                for hot, k in ((hot1, 0), (hot2, 1)):
                    nc.vector.tensor_tensor(hot[:], iota_f[:].unsqueeze(1).to_broadcast([P, XT, E]),
                                            pick[:, :, k:k + 1].to_broadcast([P, XT, E]), ALU.is_equal)
                nc.vector.reciprocal(share[:], total[:]).then_inc(gate_steps, 1)
                dve.wait_ge(gate_steps, at(6))
                nc.vector.tensor_scalar(gate1[:], share[:], SCALING, None, ALU.mult)
                nc.vector.scalar_tensor_tensor(out=gate2[:], in0=second[:], scalar=SCALING, in1=share[:],
                                               op0=ALU.mult, op1=ALU.mult).then_inc(gate_steps, 1)
                dve.wait_ge(gate_steps, at(7))
                for hot, gate in ((hot1, gate1), (hot2, gate2)):
                    last_hot = nc.vector.tensor_tensor(hot[:], hot[:], gate[:].unsqueeze(2).to_broadcast([P, XT, E]),
                                                       ALU.mult)
                last_hot.then_inc(gate_steps, 1)
                dve.wait_ge(gate_steps, at(8))
                nc.vector.tensor_tensor(gates[:], hot1[:], hot2[:], ALU.add).then_inc(gate_steps, 1)
                dve.wait_ge(gate_steps, at(9))
                nc.vector.tensor_tensor(gated[:].rearrange("p j (e r) -> p j e r", e=E),
                                        h_ps[:, :, 0:ER].rearrange("p j (e r) -> p j e r", e=E),
                                        gates[:].unsqueeze(3).to_broadcast([P, XT, E, R]),
                                        ALU.mult).then_inc(gated_ready, 1)

            def x1_low(k, ch):
                dve.wait_ge(x1_hi_done, ch * M + (k + 1))
                nc.vector.tensor_tensor(x1T_lo[:, k, :], out_ps[:, k % BANKS, :], x1T_hi[:, k, :].bitcast(F32),
                                        ALU.subtract).then_inc(x1_done, 1)

            def body(ch, last):
                make([("w", AHEAD)], ch, last)
                make_gates(ch)
                make(DURING_GATES, ch, last)
                dve.wait_ge(gT_hi_done, ch + 1)
                nc.vector.tensor_tensor(gT_lo[:], gT_ps[:], gT_hi[:].bitcast(F32), ALU.subtract).then_inc(gT_done, 1)
                for k in range(M):
                    x1_low(k, ch)
                    make(AFTER_L0[k], ch, last)
                for j in range(NH):
                    make(after_l1(j, last), ch, last)

            with dve.Fori(0, NCH - 1) as ch:
                body(ch, False)
            body(NCH - 1, True)

        @block.scalar
        def _(act):
            act.wait_ge(wr_zeroed, 1)
            for c in range(Q):
                act.dma_start(wr_raw[c * S:c * S + E, :], wr[:, c * DQ:(c + 1) * DQ]).then_inc(small_loaded, 16)
            act.dma_start(lang_i[:], lang_ids.partition_broadcast(P)).then_inc(small_loaded, 16)
            act.dma_start(adapters[:], adapter_ids.unsqueeze(0)).then_inc(adapters_loaded, 16)
            act.dma_start(b_raw, b_view).then_inc(b_loaded, 16)

            def high(item, ch, last):
                kind, n = item
                act.wait_ge(transposed, place(item, ch, last) + 1)
                if kind == "w" and ch is not None:
                    old = n - RING
                    if 0 <= old < M:
                        act.wait_ge(w0_used, ch * M + (old + 1))
                    else:
                        old_half = (old % WPC - M) // KH
                        since = 0 if old < 0 else L1_OUTS
                        act.wait_ge(l1_ready, ch * L1_OUTS + (since + (old_half + 1) * TT))
                elif kind == "x" and ch is not None:
                    act.wait_ge(w0_used, ch * M + M)
                nc.scalar.activation(dest(True, item), turned[:, slot(item, ch, last, 2)], ACT.Copy)\
                    .then_inc(hi_done, 1)

            for item in FIRST[0:2]:
                high(item, None, False)
            act.wait_ge(wr_transposed, 1)
            nc.scalar.activation(fac_hi[:, :, ER:FC], wr_turned[:, :, 0:E], ACT.Copy).then_inc(fac_hi_done, 1)
            for item in FIRST[2:6]:
                high(item, None, False)
            act.wait_ge(bT_turned, 1)
            for q in range(Q):
                src, dst = bT_slices(q)
                nc.scalar.activation(dst(bT_hi), src, ACT.Copy).then_inc(bT_hi_done, 1)
            for item in FIRST[6:]:
                high(item, None, False)
            nc.scalar.sem_inc(l1_copied, L1_OUTS)
            for s in range(OUTS):
                nc.scalar.sem_inc(stored[s], 16)

            def x1_high(k, ch):
                act.wait_ge(l0_ready, ch * M + (k + 1))
                nc.scalar.activation(x1T_hi[:, k, :], out_ps[:, k % BANKS, :], ACT.Copy).then_inc(x1_hi_done, 1)

            def put_out(j, t, ch):
                n = j * TT + t
                row, half = j // (NH // BPC), j % (NH // BPC)
                s = n % OUTS
                fill = ch * (L1_OUTS // OUTS) + n // OUTS
                act.wait_ge(l1_ready, ch * L1_OUTS + (L1_OUTS + n + 1))
                act.wait_ge(stored[s], fill * 16 + 16)
                nc.scalar.activation(out_stage[:, s, :].rearrange("p (q k s) -> p q k s", q=Q, k=KH),
                                     out_ps[:, n % BANKS, :].rearrange("p (k q s) -> p q k s", q=Q, k=KH),
                                     ACT.Copy).then_inc(l1_copied, 1)
                act.wait_ge(l1_copied, ch * L1_OUTS + (L1_OUTS + n + 1))
                dst = out_rows[bass.ds(ch * CH + (row * T + t * P), P), :]\
                    .rearrange("p (q h f) -> h p q f", q=Q, h=D // HALF)[half]
                act.dma_start(dst, out_stage[:, s, :].rearrange("p (q f) -> p q f", q=Q)).then_inc(stored[s], 16)

            def body(ch, last):
                high(("w", AHEAD), ch, last)
                act.wait_ge(drop_ready, ch + 1)
                nc.scalar.activation(second[:], drop[:], ACT.Exp).then_inc(second_ready, 1)
                for item in DURING_GATES:
                    high(item, ch, last)
                act.wait_ge(gT_turned, ch + 1)
                nc.scalar.activation(gT_hi[:], gT_ps[:], ACT.Copy).then_inc(gT_hi_done, 1)
                for k in range(M):
                    x1_high(k, ch)
                    for item in AFTER_L0[k]:
                        high(item, ch, last)
                for j in range(NH):
                    items = after_l1(j, last)
                    for t in range(TT):
                        for item in items[t * len(items) // TT:(t + 1) * len(items) // TT]:
                            high(item, ch, last)
                        put_out(j, t, ch)

            with act.Fori(0, NCH - 1) as ch:
                body(ch, False)
            body(NCH - 1, True)
            for s in range(OUTS):
                act.wait_ge(stored[s], NCH * (L1_OUTS // OUTS) * 16 + 16)

        @block.tensor
        def _(pe):
            nc.tensor.sem_inc(l1_ready, L1_OUTS)
            pe.wait_ge(consts, 3)
            pe.wait_ge(b_sorted_done, 1)
            for o in range(M):
                turn_b = nc.tensor.transpose(bT_ps[:, o * P:(o + 1) * P], b_sorted[:, o, :], ident[:])
            turn_b.then_inc(bT_turned, 1)
            pe.wait_ge(fac_done, 2)

            def products(ps, st_hi, st_lo, mv_hi, mv_lo, start, stop):
                nc.tensor.matmul(ps, st_hi, mv_hi, start=start, stop=False)
                nc.tensor.matmul(ps, st_hi, mv_lo, start=False, stop=False)
                return nc.tensor.matmul(ps, st_lo, mv_hi, start=False, stop=stop)

            def features(ch):
                for j in range(XT):
                    pe.wait_ge(x_done, ch * XT + (j + 1))
                    t = slice(j * P, (j + 1) * P)
                    for m in range(M):
                        mm = products(h_ps[:, j, 0:FC], xT_hi[:, m, t], xT_lo[:, m, t],
                                      fac_hi[:, m, :], fac_lo[:, m, :], m == 0, m == M - 1)
                mm.then_inc(h_ready, 1)

            def base_tile(k, ch):
                pe.wait_ge(w_done, ch * WPC + (k + 1))
                if k < BANKS:
                    pe.wait_ge(l1_copied, ch * L1_OUTS + (L1_OUTS - BANKS + k + 1))
                else:
                    pe.wait_ge(x1_done, ch * M + (k - BANKS + 1))
                hi, lo = ring(w_hi, k), ring(w_lo, k)
                for m in range(M):
                    mm = products(out_ps[:, k % BANKS, :], hi[:, m, :], lo[:, m, :], xT_hi[:, m, :], xT_lo[:, m, :],
                                  m == 0, False)
                mm.then_inc(w0_used, 1)

            def lora_tile(k):
                c = slice(k * P, (k + 1) * P)
                products(out_ps[:, k % BANKS, :], bT_hi[:, c], bT_lo[:, c], gT_hi[:], gT_lo[:], False, True)\
                    .then_inc(l0_ready, 1)

            def body(ch, last):
                features(ch)
                for k in range(2):
                    base_tile(k, ch)
                pe.wait_ge(gated_ready, ch + 1)
                for j in range(XT):
                    turn_g = nc.tensor.transpose(gT_ps[:, j * P:(j + 1) * P], gated[:, j, :], ident[:])
                turn_g.then_inc(gT_turned, 1)
                pe.wait_ge(bT_done, Q)
                pe.wait_ge(gT_done, ch + 1)
                for k in range(2):
                    lora_tile(k)
                for k in range(2, M):
                    base_tile(k, ch)
                    lora_tile(k)
                for j in range(NH):
                    row, g = j // (NH // BPC), (M // KH + j) % GROUPS
                    pe.wait_ge(w_done, ch * WPC + (M + (j + 1) * KH))
                    for t in range(TT):
                        n = j * TT + t
                        if n >= BANKS:
                            pe.wait_ge(l1_copied, ch * L1_OUTS + (L1_OUTS + n - BANKS + 1))
                        tok = slice(row * T + t * P, row * T + (t + 1) * P)
                        for m in range(M):
                            if j == 0 and t == 0:
                                pe.wait_ge(x1_done, ch * M + max(m + 1, M - BANKS + 1))
                            mm = products(out_ps[:, n % BANKS, :], x1T_hi[:, m, tok], x1T_lo[:, m, tok],
                                          w_hi[:, g, m, :], w_lo[:, g, m, :], m == 0, m == M - 1)
                        mm.then_inc(l1_ready, 1)

            with pe.Fori(0, NCH - 1) as ch:
                body(ch, False)
            body(NCH - 1, True)


_INS = ['x', 'itok_B_0_7', 'itok_B_0_15', 'L0_cond_W', 'L0_cond_Wr', 'L0_cond_A', 'L0_cond_B', 'L1_cond_weight']
_OUTS = [((8, 256, 1024), 'float32')]


def kernel(**inputs):
    import numpy as _np
    import concourse.bacc as _bacc
    from concourse import mybir as _mybir
    from concourse.bass_utils import run_bass_kernel_spmd as _run

    nc = _bacc.Bacc("TRN2", target_bir_lowering=False, num_devices=1, dynamic_dma_scratch_size=1024)
    arrays, args = {}, []
    for name in _INS:
        a = _np.ascontiguousarray(inputs[name])
        arrays[f"in_{name}_dram"] = a
        args.append(nc.dram_tensor(f"in_{name}_dram", a.shape, _mybir.dt.from_np(a.dtype), kind="ExternalInput").ap())
    for i, (shape, dtype) in enumerate(_OUTS):
        dt = _mybir.dt.from_np(_np.dtype(dtype))
        args.append(nc.dram_tensor(f"out_{i}_dram", shape, dt, kind="ExternalOutput").ap())
    cond_resid_kernel(nc, *args)
    r = _run(nc, [arrays], core_ids=[0])
    got = tuple(r.results[0][f"out_{i}_dram"] for i in range(len(_OUTS)))
    return got[0]
```

```python
import concourse.bass as bass
from concourse import mybir
from contextlib import ExitStack


def cond_resid_kernel(nc, x, lang_ids, adapter_ids, w0, wr, a, b, w1, out):
    F32 = mybir.dt.float32
    F32R = mybir.dt.float32r
    I32 = mybir.dt.int32
    U32 = mybir.dt.uint32
    ALU = mybir.AluOpType
    ACT = mybir.ActivationFunctionType

    NB, T, D = x.shape
    E, R, _ = a.shape
    NA = w1.shape[0]
    P = 128
    Q = 4
    S = P // Q
    DQ = D // Q
    M = D // P
    CH = 512
    NCH = NB * T // CH
    BPC = CH // T
    XT = CH // P
    TT = T // P
    HALF = 512
    KH = HALF // P
    NH = BPC * M // KH
    ER = E * R
    FC = ER + E
    LANG_BIAS = 5.0
    SCALING = 2.0

    WPC = M + BPC * M
    GROUPS = 3
    RING = GROUPS * KH
    RAW = 4
    BANKS = 7
    WARM = 37
    OUTS = 4
    L1_OUTS = NH * TT
    assert WPC % RING == 0 and ER == P and L1_OUTS % OUTS == 0 and M == 8 and L1_OUTS == 8

    AHEAD = 3
    FIRST = [("x", 0), ("a", 0)] + [("x", j) for j in range(1, XT)] + [("w", 0), ("w", 1), ("w", 2), ("b", 0)]
    AFTER_GATES = [("w", 3), ("w", 4)]
    AFTER_GATED = [("w", 5), ("w", 6), ("w", 7)]
    AFTER_L0 = [[], [], [("w", 8), ("w", 9)], [("w", 10), ("w", 11)], [("w", 12), ("w", 13)], [("w", 14), ("w", 15)],
                [("w", 16), ("w", 17)], []]

    def after_l1(j, last):
        own = [[18, 19], [20, 21], [22, 23], []][j]
        tokens = [[0, 1], [2, 3], [], []][j]
        following = [[], [], [0, 1], [2]][j]
        return [("w", n) for n in own] + ([] if last else [("x", t) for t in tokens] +
                                          [("w", WPC + n) for n in following])

    def body_order(last):
        return (AFTER_GATES + AFTER_GATED + [t for l in AFTER_L0 for t in l] +
                [t for j in range(NH) for t in after_l1(j, last)])

    N_FIRST = len(FIRST)
    N_BODY = len(body_order(False))
    assert N_BODY % RAW == 0 and N_BODY == WPC + XT
    assert FIRST[-2:] == [("w", AHEAD - 1), ("b", 0)] and body_order(False)[-1] == ("w", WPC + AHEAD - 1)
    POS = {False: {t: i for i, t in enumerate(body_order(False))},
           True: {t: i for i, t in enumerate(body_order(True))}}
    FIRST_POS = {t: i for i, t in enumerate(FIRST)}

    x_rows = x.rearrange("n t d -> (n t) d")
    out_rows = out.rearrange("n t d -> (n t) d")
    a_rows = a.rearrange("e r d -> (e r) d")
    w1_rows = w1.rearrange("n o i -> (n o) i")
    b_pairs = b.rearrange("(c e) (s k) r -> c s e (k r)", c=Q, s=S)

    ctx = ExitStack()
    with ctx:
        def sb(name, shape, dt=F32):
            return ctx.enter_context(nc.sbuf_tensor(name, shape, dt))

        def pb(name, shape):
            return ctx.enter_context(nc.psum_tensor(name, shape, F32))

        def sem(name):
            return ctx.enter_context(nc.semaphore(name))

        xT_hi, xT_lo = sb("xT_hi", [P, M, CH], F32R), sb("xT_lo", [P, M, CH], F32R)
        x1T_hi, x1T_lo = sb("x1T_hi", [P, M, CH], F32R), sb("x1T_lo", [P, M, CH], F32R)
        w_hi, w_lo = sb("w_hi", [P, GROUPS, M, HALF], F32R), sb("w_lo", [P, GROUPS, M, HALF], F32R)
        fac = sb("fac", [P, M, 2, FC], F32R)
        bT_hi, bT_lo = sb("bT_hi", [ER, D], F32R), sb("bT_lo", [ER, D], F32R)
        gT_hi, gT_lo = sb("gT_hi", [ER, CH], F32R), sb("gT_lo", [ER, CH], F32R)
        raw = sb("raw", [P, RAW, D])
        turned = sb("turned", [P, 2, M, P])
        out_stage = sb("out_stage", [P, OUTS, HALF])
        wr_turned = sb("wr_turned", [P, M, S])
        ident = sb("ident", [P, P])
        iota_i = sb("iota_i", [P, E], I32)
        iota_f = sb("iota_f", [P, E])
        lang_i = sb("lang_i", [P, NB], I32)
        lang_f = sb("lang_f", [P, NB])
        bias = sb("bias", [P, NB, E])
        adapters = sb("adapters", [1, NB], I32)
        logits = sb("logits", [P, XT, E])
        top = sb("top", [P, XT, 8])
        top_i = sb("top_i", [P, XT, 8], U32)
        pick = sb("pick", [P, XT, 2])
        largest = sb("largest", [P, XT])
        drop = sb("drop", [P, XT])
        second = sb("second", [P, XT])
        total = sb("total", [P, XT])
        share = sb("share", [P, XT])
        gate1 = sb("gate1", [P, XT])
        gate2 = sb("gate2", [P, XT])
        hot1 = sb("hot1", [P, XT, E])
        hot2 = sb("hot2", [P, XT, E])
        gates = sb("gates", [P, XT, E])
        h = sb("h", [P, XT, FC])
        gated = sb("gated", [P, XT, ER])
        wr_raw = gated[:, 0:2, :].rearrange("p j f -> p (j f)")

        banks = pb("banks", [P, BANKS, HALF])
        gT_ps = pb("gT_ps", [ER, CH])
        h_ps = banks[:, 0:XT, 0:2 * FC].rearrange("p j (s f) -> p j s f", s=2)

        def l0_bank(k):
            return (XT + k) % BANKS

        def l1_bank(n):
            return (XT + M + n) % BANKS

        raw_loaded = [sem(f"raw_loaded{s}") for s in range(RAW)]
        wr_loaded = sem("wr_loaded")
        lang_loaded = sem("lang_loaded")
        adapters_loaded = sem("adapters_loaded")
        wr_zeroed = sem("wr_zeroed")
        consts = sem("consts")
        ones_added = sem("ones_added")
        transposed = sem("transposed")
        wr_transposed = sem("wr_transposed")
        hi_done = sem("hi_done")
        x_done = sem("x_done")
        w_done = sem("w_done")
        fac_hi_done = sem("fac_hi_done")
        fac_done = sem("fac_done")
        bT_done = sem("bT_done")
        w0_used = sem("w0_used")
        h_ready = sem("h_ready")
        h_lo_copied = sem("h_lo_copied")
        gate_steps = sem("gate_steps")
        drop_ready = sem("drop_ready")
        second_ready = sem("second_ready")
        gated_ready = sem("gated_ready")
        gT_turned = sem("gT_turned")
        gT_hi_done = sem("gT_hi_done")
        gT_done = sem("gT_done")
        l0_ready = sem("l0_ready")
        x1_hi_done = sem("x1_hi_done")
        x1_done = sem("x1_done")
        l1_ready = sem("l1_ready")
        l1_copied = sem("l1_copied")
        stored = [sem(f"stored{s}") for s in range(OUTS)]
        setup = sem("setup")

        GATE_STEPS = 10

        def place(item, ch, last):
            return FIRST_POS[item] if ch is None else ch * N_BODY + (N_FIRST + POS[last][item])

        def slot(item, ch, last, n):
            return (FIRST_POS[item] if ch is None else N_FIRST + POS[last][item]) % n

        def fills(item, ch, last):
            if ch is None:
                return FIRST_POS[item] // RAW + 1
            return ch * (N_BODY // RAW) + ((N_FIRST + POS[last][item]) // RAW + 1)

        def base(ch):
            return 0 if ch is None else ch

        def ring(t, n):
            s = n % RING
            return t[:, s // KH, :, (s % KH) * P:(s % KH + 1) * P]

        def dest(hi, item):
            kind, n = item
            if kind == "x":
                return (xT_hi if hi else xT_lo)[:, :, n * P:(n + 1) * P]
            if kind == "b":
                return (bT_hi if hi else bT_lo)[:].rearrange("p (m f) -> p m f", m=M)
            if kind == "a":
                return fac[:, :, 0 if hi else 1, 0:ER]
            return ring(w_hi if hi else w_lo, n)

        block = ctx.enter_context(nc.Block())

        @block.sync
        def _(sp):
            def rows(item, ch, ids):
                kind, n = item
                if kind == "a":
                    return a_rows[:, :].rearrange("(q s) d -> s q d", s=S)
                if kind == "x":
                    t0 = n * P if ch is None else ch * CH + (CH + n * P)
                    return x_rows[bass.ds(t0, P), :].rearrange("(q s) d -> s q d", s=S)
                if n < M or n >= WPC:
                    return w0.rearrange("(q m s) d -> m s q d", m=M, s=S)[n % WPC]
                row, m = (n - M) // M, (n - M) % M
                return w1_rows[bass.ds(ids[row] * D, D), :].rearrange("(q m s) d -> m s q d", m=M, s=S)[m]

            def load(item, ch, last, ids=None):
                s = slot(item, ch, last, RAW)
                n = place(item, ch, last)
                if ch is not None or n >= RAW:
                    sp.wait_ge(transposed, n - (RAW - 1))
                src = None if item[0] == "b" else rows(item, ch, ids)
                for c in range(Q):
                    if src is None:
                        sp.dma_start(raw[c * S:(c + 1) * S, s, :].rearrange("p (e f) -> p e f", e=E // Q),
                                     b_pairs[c]).then_inc(raw_loaded[s], 16)
                        continue
                    sp.dma_start(raw[c * S:(c + 1) * S, s, :].rearrange("p (q j) -> p q j", q=Q),
                                 src[:, :, c * DQ:(c + 1) * DQ]).then_inc(raw_loaded[s], 16)

            for item in FIRST:
                load(item, None, False)
                if item == ("x", 0):
                    sp.dma_start(lang_i[:], lang_ids.partition_broadcast(P)).then_inc(lang_loaded, 16)
                elif item == ("x", 1):
                    sp.wait_ge(wr_zeroed, 1)
                    for c in range(Q):
                        sp.dma_start(wr_raw[c * S:c * S + E, :], wr[:, c * DQ:(c + 1) * DQ]).then_inc(wr_loaded, 16)
                elif item == ("w", 0):
                    sp.dma_start(adapters[:], adapter_ids.unsqueeze(0)).then_inc(adapters_loaded, 16)
            sp.wait_ge(adapters_loaded, 16)

            def body(ch, last):
                ids = [sp.value_load(adapters[0:1, bass.ds(ch * BPC + r, 1)], min_val=0, max_val=NA - 1)
                       for r in range(BPC)]
                for item in body_order(last):
                    load(item, ch, last, ids)

            with sp.Fori(0, NCH - 1) as ch:
                body(ch, False)
            body(NCH - 1, True)

        @block.gpsimd
        def _(pool):
            nc.gpsimd.memset(wr_raw, 0.0).then_inc(wr_zeroed, 1)
            nc.gpsimd.memset(ident[:], 0.0).then_inc(consts, 1)
            nc.gpsimd.iota(iota_i[:], [[1, E]], base=0, channel_multiplier=0).then_inc(consts, 1)
            pool.wait_ge(consts, 1)
            nc.gpsimd.affine_select(out=ident[:], in_=ident[:], compare_op=ALU.not_equal, fill=1.0, base=0,
                                    pattern=[[-1, P]], channel_multiplier=1).then_inc(consts, 1)
            pool.wait_ge(consts, 3)

            def add_ones(item, ch, last):
                kind, n = item
                if kind != "w":
                    return
                m = n % WPC % M
                s = slot(item, ch, last, RAW)
                spot = raw[:, s, :].rearrange("p (q j) -> p q j", q=Q)[:, :, m * S:(m + 1) * S]
                pool.wait_ge(raw_loaded[s], fills(item, ch, last) * (Q * 16))
                nc.gpsimd.tensor_tensor(spot, spot, ident[:].rearrange("p (q j) -> p q j", q=Q), ALU.add)\
                    .then_inc(ones_added, 1)

            for item in FIRST:
                add_ones(item, None, False)

            def body(ch, last):
                for item in body_order(last):
                    add_ones(item, ch, last)

            with pool.Fori(0, NCH - 1) as ch:
                body(ch, False)
            body(NCH - 1, True)

        @block.vector
        def _(dve):
            def two_before(item, ch, last):
                order, at = (FIRST, FIRST_POS[item]) if ch is None else (body_order(last), POS[last][item])
                if at < 2:
                    return [] if ch is None else [("w", AHEAD - 1)] + [("b", 0)] * at
                return [order[at - 2]]

            def made(item, ch):
                kind, n = item
                if kind == "w":
                    dve.wait_ge(w_done, base(ch) * WPC + (n + 1))
                elif kind == "x":
                    dve.wait_ge(x_done, n + 1 if ch is None else ch * XT + (XT + n + 1))
                else:
                    dve.wait_ge({"a": fac_done, "b": bT_done}[kind], 1)

            def turn(item, ch, last):
                kind, n = item
                s = slot(item, ch, last, RAW)
                if kind == "w":
                    dve.wait_ge(ones_added, base(ch) * WPC + (n + 1))
                else:
                    dve.wait_ge(raw_loaded[s], fills(item, ch, last) * (Q * 16))
                for old in two_before(item, ch, last):
                    made(old, ch)
                if kind == "b":
                    nc.vector.transpose(turned[:, slot(item, ch, last, 2)].rearrange("p m (q k) -> p k q m", q=Q),
                                        raw[:, s, :].rearrange("p (e k r) -> p k e r", e=E // Q, r=R))\
                        .then_inc(transposed, 1)
                    return
                nc.vector.transpose(turned[:, slot(item, ch, last, 2)].rearrange("p m (q s) -> p q m s", q=Q),
                                    raw[:, s, :].rearrange("p (q m j) -> p q m j", q=Q, m=M))\
                    .then_inc(transposed, 1)

            def low(item, ch, last):
                kind, n = item
                dve.wait_ge(hi_done, place(item, ch, last) + 1)
                nc.vector.tensor_tensor(dest(False, item), turned[:, slot(item, ch, last, 2)],
                                        dest(True, item).bitcast(F32), ALU.subtract)\
                    .then_inc({"x": x_done, "w": w_done, "a": fac_done, "b": bT_done}[kind], 1)

            def make(items, ch, last):
                for before, item in zip([None] + items, items + [None]):
                    if item:
                        turn(item, ch, last)
                    if before:
                        low(before, ch, last)

            x0, fac_a, x1, x2, x3, first_w = FIRST[0:6]
            turn(x0, None, False)
            dve.wait_ge(consts, 3)
            nc.vector.tensor_copy(iota_f[:], iota_i[:]).then_inc(setup, 1)
            dve.wait_ge(lang_loaded, 16)
            nc.vector.tensor_copy(lang_f[:], lang_i[:]).then_inc(setup, 1)
            dve.wait_ge(setup, 2)
            nc.vector.tensor_tensor(bias[:], iota_f[:].unsqueeze(1).to_broadcast([P, NB, E]),
                                    lang_f[:].unsqueeze(2).to_broadcast([P, NB, E]), ALU.is_equal).then_inc(setup, 1)
            turn(fac_a, None, False)
            low(x0, None, False)
            dve.wait_ge(setup, 3)
            nc.vector.tensor_scalar(bias[:], bias[:], LANG_BIAS, None, ALU.mult).then_inc(setup, 1)
            turn(x1, None, False)
            low(fac_a, None, False)
            dve.wait_ge(wr_loaded, Q * 16)
            nc.vector.transpose(wr_turned[:], wr_raw.rearrange("p (m j) -> p m j", m=M)).then_inc(wr_transposed, 1)
            low(x1, None, False)
            dve.wait_ge(fac_hi_done, 1)
            nc.vector.tensor_tensor(fac[:, :, 1, ER:FC], wr_turned[:, :, 0:E], fac[:, :, 0, ER:FC].bitcast(F32),
                                    ALU.subtract).then_inc(fac_done, 1)
            make([x2, x3, first_w], None, False)
            make(FIRST[6:-1], None, False)
            dve.wait_ge(setup, 4)

            def make_gates(ch):
                at = lambda k: ch * GATE_STEPS + k
                dve.wait_ge(h_lo_copied, ch + 1)
                nc.vector.tensor_tensor(h[:], h_ps[:, :, 0, :], h[:], ALU.add).then_inc(gate_steps, 1)
                dve.wait_ge(gate_steps, at(1))
                nc.vector.tensor_tensor(
                    logits[:].rearrange("p (r t) e -> p r t e", r=BPC),
                    h[:, :, ER:FC].rearrange("p (r t) e -> p r t e", r=BPC),
                    bias[:, bass.ds(ch * BPC, BPC), :].unsqueeze(2).to_broadcast([P, BPC, TT, E]),
                    ALU.add).then_inc(gate_steps, 1)
                dve.wait_ge(gate_steps, at(2))
                nc.vector.tensor_reduce(largest[:], logits[:], mybir.AxisListType.X, ALU.max)
                for j in range(XT):
                    last_max = nc.vector.max(top[:, j, :], logits[:, j, :])
                last_max.then_inc(gate_steps, 1)
                dve.wait_ge(gate_steps, at(3))
                nc.vector.tensor_tensor(drop[:], top[:, :, 1], largest[:], ALU.subtract).then_inc(drop_ready, 1)
                for j in range(XT):
                    last_index = nc.vector.max_index(top_i[:, j, :], top[:, j, :], logits[:, j, :])
                last_index.then_inc(gate_steps, 1)
                dve.wait_ge(gate_steps, at(4))
                nc.vector.tensor_copy(pick[:], top_i[:, :, 0:2]).then_inc(gate_steps, 1)
                dve.wait_ge(second_ready, ch + 1)
                nc.vector.tensor_scalar(total[:], second[:], 1.0, None, ALU.add).then_inc(gate_steps, 1)
                dve.wait_ge(gate_steps, at(6))
                for hot, k in ((hot1, 0), (hot2, 1)):
                    nc.vector.tensor_tensor(hot[:], iota_f[:].unsqueeze(1).to_broadcast([P, XT, E]),
                                            pick[:, :, k:k + 1].to_broadcast([P, XT, E]), ALU.is_equal)
                nc.vector.reciprocal(share[:], total[:]).then_inc(gate_steps, 1)
                dve.wait_ge(gate_steps, at(7))
                nc.vector.tensor_scalar(gate1[:], share[:], SCALING, None, ALU.mult)
                nc.vector.scalar_tensor_tensor(out=gate2[:], in0=second[:], scalar=SCALING, in1=share[:],
                                               op0=ALU.mult, op1=ALU.mult).then_inc(gate_steps, 1)
                dve.wait_ge(gate_steps, at(8))
                for hot, gate in ((hot1, gate1), (hot2, gate2)):
                    last_hot = nc.vector.tensor_tensor(hot[:], hot[:], gate[:].unsqueeze(2).to_broadcast([P, XT, E]),
                                                       ALU.mult)
                last_hot.then_inc(gate_steps, 1)
                dve.wait_ge(gate_steps, at(9))
                nc.vector.tensor_tensor(gates[:], hot1[:], hot2[:], ALU.add).then_inc(gate_steps, 1)
                dve.wait_ge(gate_steps, at(10))
                nc.vector.tensor_tensor(gated[:].rearrange("p j (e r) -> p j e r", e=E),
                                        h[:, :, 0:ER].rearrange("p j (e r) -> p j e r", e=E),
                                        gates[:].unsqueeze(3).to_broadcast([P, XT, E, R]),
                                        ALU.mult).then_inc(gated_ready, 1)

            def x1_low(k, ch):
                dve.wait_ge(x1_hi_done, ch * M + (k + 1))
                nc.vector.tensor_tensor(x1T_lo[:, k, :], banks[:, l0_bank(k), :], x1T_hi[:, k, :].bitcast(F32),
                                        ALU.subtract).then_inc(x1_done, 1)

            def body(ch, last):
                make(AFTER_GATES, ch, last)
                dve.wait_ge(gT_hi_done, ch + 1)
                nc.vector.tensor_tensor(gT_lo[:], gT_ps[:], gT_hi[:].bitcast(F32), ALU.subtract).then_inc(gT_done, 1)
                make(AFTER_GATED, ch, last)
                for k in range(M):
                    x1_low(k, ch)
                    make(AFTER_L0[k], ch, last)
                for j in range(NH):
                    make(after_l1(j, last), ch, last)
                if not last:
                    make_gates(ch + 1)

            turn(FIRST[-1], None, False)
            make_gates(0)
            low(FIRST[-1], None, False)

            with dve.Fori(0, NCH - 1) as ch:
                body(ch, False)
            body(NCH - 1, True)

        @block.scalar
        def _(act):
            nc.scalar.sem_inc(l1_copied, L1_OUTS)
            for s in range(OUTS):
                nc.scalar.sem_inc(stored[s], 16)

            def high(item, ch, last):
                kind, n = item
                act.wait_ge(transposed, place(item, ch, last) + 1)
                if kind == "w" and ch is not None:
                    old = n - RING
                    if 0 <= old < M:
                        act.wait_ge(w0_used, ch * M + (old + 1))
                    else:
                        old_half = (old % WPC - M) // KH
                        since = 0 if old < 0 else L1_OUTS
                        act.wait_ge(l1_ready, ch * L1_OUTS + (since + (old_half + 1) * TT))
                elif kind == "x" and ch is not None:
                    act.wait_ge(w0_used, ch * M + M)
                nc.scalar.activation(dest(True, item), turned[:, slot(item, ch, last, 2)], ACT.Copy)\
                    .then_inc(hi_done, 1)

            for item in FIRST[0:3]:
                high(item, None, False)
            act.wait_ge(wr_transposed, 1)
            nc.scalar.activation(fac[:, :, 0, ER:FC], wr_turned[:, :, 0:E], ACT.Copy).then_inc(fac_hi_done, 1)
            for item in FIRST[3:-1]:
                high(item, None, False)

            def copy_h(ch):
                act.wait_ge(h_ready, ch + 1)
                nc.scalar.activation(h[:], h_ps[:, :, 1, :], ACT.Copy).then_inc(h_lo_copied, 1)

            def exponentials(ch):
                act.wait_ge(drop_ready, ch + 1)
                nc.scalar.activation(second[:], drop[:], ACT.Exp).then_inc(second_ready, 1)

            def x1_high(k, ch):
                act.wait_ge(l0_ready, ch * M + (k + 1))
                nc.scalar.activation(x1T_hi[:, k, :], banks[:, l0_bank(k), :], ACT.Copy).then_inc(x1_hi_done, 1)

            def put_out(j, t, ch):
                n = j * TT + t
                row, half = j // (NH // BPC), j % (NH // BPC)
                s = n % OUTS
                fill = ch * (L1_OUTS // OUTS) + n // OUTS
                act.wait_ge(l1_ready, ch * L1_OUTS + (L1_OUTS + n + 1))
                act.wait_ge(stored[s], fill * 16 + 16)
                nc.scalar.activation(out_stage[:, s, :].rearrange("p (q k s) -> p q k s", q=Q, k=KH),
                                     banks[:, l1_bank(n), :].rearrange("p (k q s) -> p q k s", q=Q, k=KH),
                                     ACT.Copy).then_inc(l1_copied, 1)
                act.wait_ge(l1_copied, ch * L1_OUTS + (L1_OUTS + n + 1))
                dst = out_rows[bass.ds(ch * CH + (row * T + t * P), P), :]\
                    .rearrange("p (q h f) -> h p q f", q=Q, h=D // HALF)[half]
                act.dma_start(dst, out_stage[:, s, :].rearrange("p (q f) -> p q f", q=Q)).then_inc(stored[s], 16)

            def body(ch, last):
                for item in AFTER_GATES:
                    high(item, ch, last)
                act.wait_ge(gT_turned, ch + 1)
                nc.scalar.activation(gT_hi[:], gT_ps[:], ACT.Copy).then_inc(gT_hi_done, 1)
                for item in AFTER_GATED:
                    high(item, ch, last)
                for k in range(M):
                    x1_high(k, ch)
                    for item in AFTER_L0[k]:
                        high(item, ch, last)
                for j in range(NH):
                    items = after_l1(j, last)
                    for t in range(TT):
                        for item in items[t * len(items) // TT:(t + 1) * len(items) // TT]:
                            high(item, ch, last)
                        put_out(j, t, ch)
                if not last:
                    copy_h(ch + 1)
                    exponentials(ch + 1)

            copy_h(0)
            high(FIRST[-1], None, False)
            exponentials(0)
            with act.Fori(0, NCH - 1) as ch:
                body(ch, False)
            body(NCH - 1, True)
            for s in range(OUTS):
                act.wait_ge(stored[s], NCH * (L1_OUTS // OUTS) * 16 + 16)

        @block.tensor
        def _(pe):
            nc.tensor.sem_inc(l1_ready, L1_OUTS)
            pe.wait_ge(consts, 3)
            for _ in range(WARM):
                nc.tensor.matmul(gT_ps[:, 0:P], ident[:], ident[:], start=True, stop=True)
            def products(ps, st_hi, st_lo, mv_hi, mv_lo, start, stop):
                nc.tensor.matmul(ps, st_hi, mv_hi, start=start, stop=False)
                nc.tensor.matmul(ps, st_hi, mv_lo, start=False, stop=False)
                return nc.tensor.matmul(ps, st_lo, mv_hi, start=False, stop=stop)

            def features(ch):
                pe.wait_ge(fac_done, 2)
                for j in range(XT):
                    n = (j - XT - M) % BANKS
                    pe.wait_ge(l1_copied, ch * L1_OUTS + (n + 1))
                    pe.wait_ge(x_done, ch * XT + (j + 1))
                    t = slice(j * P, (j + 1) * P)
                    for m in range(M):
                        nc.tensor.matmul(banks[:, j, 0:2 * FC], xT_hi[:, m, t],
                                         fac[:, m, :, :].rearrange("p s f -> p (s f)"), start=m == 0, stop=False)
                        mm = nc.tensor.matmul(banks[:, j, 0:FC], xT_lo[:, m, t], fac[:, m, 0, :],
                                              start=False, stop=m == M - 1)
                mm.then_inc(h_ready, 1)

            def base_tile(k, ch):
                pe.wait_ge(w_done, ch * WPC + (k + 1))
                old = k + XT - BANKS
                if old < 0:
                    n = max(n for n in range(L1_OUTS) if l1_bank(n) == l0_bank(k))
                    pe.wait_ge(l1_copied, ch * L1_OUTS + (n + 1))
                elif old < XT:
                    pe.wait_ge(gate_steps, ch * GATE_STEPS + 1)
                else:
                    pe.wait_ge(x1_done, ch * M + (old - XT + 1))
                hi, lo = ring(w_hi, k), ring(w_lo, k)
                for m in range(M):
                    mm = products(banks[:, l0_bank(k), :], hi[:, m, :], lo[:, m, :], xT_hi[:, m, :], xT_lo[:, m, :],
                                  m == 0, False)
                mm.then_inc(w0_used, 1)

            def lora_tile(k):
                c = slice(k * P, (k + 1) * P)
                products(banks[:, l0_bank(k), :], bT_hi[:, c], bT_lo[:, c], gT_hi[:], gT_lo[:], False, True)\
                    .then_inc(l0_ready, 1)

            def body(ch, last):
                features(ch)
                base_tile(0, ch)
                base_tile(1, ch)
                pe.wait_ge(gated_ready, ch + 1)
                for j in range(XT):
                    turn_g = nc.tensor.transpose(gT_ps[:, j * P:(j + 1) * P], gated[:, j, :], ident[:])
                turn_g.then_inc(gT_turned, 1)
                base_tile(2, ch)
                pe.wait_ge(bT_done, 1)
                pe.wait_ge(gT_done, ch + 1)
                for k in range(3):
                    lora_tile(k)
                for k in range(3, M):
                    base_tile(k, ch)
                    lora_tile(k)
                for j in range(NH):
                    row, g = j // (NH // BPC), (M // KH + j) % GROUPS
                    pe.wait_ge(w_done, ch * WPC + (M + (j + 1) * KH))
                    for t in range(TT):
                        n = j * TT + t
                        if n >= BANKS:
                            pe.wait_ge(l1_copied, ch * L1_OUTS + (L1_OUTS + n - BANKS + 1))
                        tok = slice(row * T + t * P, row * T + (t + 1) * P)
                        for m in range(M):
                            if j == 0 and t == 0:
                                pe.wait_ge(x1_done, ch * M + max(m + 1, M - BANKS + 1))
                            mm = products(banks[:, l1_bank(n), :], x1T_hi[:, m, tok], x1T_lo[:, m, tok],
                                          w_hi[:, g, m, :], w_lo[:, g, m, :], m == 0, m == M - 1)
                        mm.then_inc(l1_ready, 1)

            with pe.Fori(0, NCH - 1) as ch:
                body(ch, False)
            body(NCH - 1, True)


_INS = ['x', 'itok_B_0_7', 'itok_B_0_15', 'L0_cond_W', 'L0_cond_Wr', 'L0_cond_A', 'L0_cond_B', 'L1_cond_weight']
_OUTS = [((8, 256, 1024), 'float32')]


def kernel(**inputs):
    import numpy as _np
    import concourse.bacc as _bacc
    from concourse import mybir as _mybir
    from concourse.bass_utils import run_bass_kernel_spmd as _run

    nc = _bacc.Bacc("TRN2", target_bir_lowering=False, num_devices=1, dynamic_dma_scratch_size=1024)
    arrays, args = {}, []
    for name in _INS:
        a = _np.ascontiguousarray(inputs[name])
        arrays[f"in_{name}_dram"] = a
        args.append(nc.dram_tensor(f"in_{name}_dram", a.shape, _mybir.dt.from_np(a.dtype), kind="ExternalInput").ap())
    for i, (shape, dtype) in enumerate(_OUTS):
        dt = _mybir.dt.from_np(_np.dtype(dtype))
        args.append(nc.dram_tensor(f"out_{i}_dram", shape, dt, kind="ExternalOutput").ap())
    cond_resid_kernel(nc, *args)
    r = _run(nc, [arrays], core_ids=[0])
    got = tuple(r.results[0][f"out_{i}_dram"] for i in range(len(_OUTS)))
    return got[0]
```
